# Optimizing a Trainium2 kernel written in Bass

```python
import numpy as np
import jax
import jax.numpy as jnp

def _softmax(x, axis=-1):
    return jax.nn.softmax(x, axis=axis)

def _gelu(x):
    return jax.nn.gelu(x, approximate=True)

def _silu(x):
    return jax.nn.silu(x)

def _sigmoid(x):
    return jax.nn.sigmoid(x)

def _layernorm(x, axis=-1, eps=1e-05):
    m = jnp.mean(x, axis=axis, keepdims=True)
    v = jnp.var(x, axis=axis, keepdims=True)
    return (x - m) / jnp.sqrt(v + eps)

def _scatter_add(tgt, idx, src, axis=0):
    return tgt.at[idx].add(src)

def _segment_sum(src, seg, n):
    return jax.ops.segment_sum(src, seg, n)
kernel_name = 'mk_dlrm_tower_d1_rec_r8_db30f1'

def setup_inputs(seed: int=0):
    np.random.seed(seed)
    _w = jnp.asarray

    def _rec_inputs():
        import jax
        import jax.numpy as jnp
        _tk = jax.random.key(seed)
        dense_ctx = jax.random.normal(jax.random.fold_in(_tk, 190), (512, 16), jnp.float32)
        ids = jnp.stack([jax.random.randint(jax.random.fold_in(_tk, 200 + f), (512,), 0, v, jnp.int32) for f, v in enumerate([1000, 1250, 1000, 1000, 1000, 1000, 1000, 12500, 1250, 1250, 1000, 12500, 1250, 1000, 1000, 1250, 1250, 1000, 1250, 1250, 1000, 12500, 1000, 1000, 1250, 1000, 1000, 12500, 1000, 1250, 1000, 1000])], axis=1)
        tbl_0 = 0.05 * jax.random.normal(jax.random.fold_in(_tk, 500 + 0), (1000, 256), jnp.float32)
        tbl_1 = 0.05 * jax.random.normal(jax.random.fold_in(_tk, 500 + 1), (1250, 256), jnp.float32)
        tbl_2 = 0.05 * jax.random.normal(jax.random.fold_in(_tk, 500 + 2), (1000, 256), jnp.float32)
        tbl_3 = 0.05 * jax.random.normal(jax.random.fold_in(_tk, 500 + 3), (1000, 256), jnp.float32)
        tbl_4 = 0.05 * jax.random.normal(jax.random.fold_in(_tk, 500 + 4), (1000, 256), jnp.float32)
        tbl_5 = 0.05 * jax.random.normal(jax.random.fold_in(_tk, 500 + 5), (1000, 256), jnp.float32)
        tbl_6 = 0.05 * jax.random.normal(jax.random.fold_in(_tk, 500 + 6), (1000, 256), jnp.float32)
        tbl_7 = 0.05 * jax.random.normal(jax.random.fold_in(_tk, 500 + 7), (12500, 256), jnp.float32)
        tbl_8 = 0.05 * jax.random.normal(jax.random.fold_in(_tk, 500 + 8), (1250, 256), jnp.float32)
        tbl_9 = 0.05 * jax.random.normal(jax.random.fold_in(_tk, 500 + 9), (1250, 256), jnp.float32)
        tbl_10 = 0.05 * jax.random.normal(jax.random.fold_in(_tk, 500 + 10), (1000, 256), jnp.float32)
        tbl_11 = 0.05 * jax.random.normal(jax.random.fold_in(_tk, 500 + 11), (12500, 256), jnp.float32)
        tbl_12 = 0.05 * jax.random.normal(jax.random.fold_in(_tk, 500 + 12), (1250, 256), jnp.float32)
        tbl_13 = 0.05 * jax.random.normal(jax.random.fold_in(_tk, 500 + 13), (1000, 256), jnp.float32)
        tbl_14 = 0.05 * jax.random.normal(jax.random.fold_in(_tk, 500 + 14), (1000, 256), jnp.float32)
        tbl_15 = 0.05 * jax.random.normal(jax.random.fold_in(_tk, 500 + 15), (1250, 256), jnp.float32)
        tbl_16 = 0.05 * jax.random.normal(jax.random.fold_in(_tk, 500 + 16), (1250, 256), jnp.float32)
        tbl_17 = 0.05 * jax.random.normal(jax.random.fold_in(_tk, 500 + 17), (1000, 256), jnp.float32)
        tbl_18 = 0.05 * jax.random.normal(jax.random.fold_in(_tk, 500 + 18), (1250, 256), jnp.float32)
        tbl_19 = 0.05 * jax.random.normal(jax.random.fold_in(_tk, 500 + 19), (1250, 256), jnp.float32)
        tbl_20 = 0.05 * jax.random.normal(jax.random.fold_in(_tk, 500 + 20), (1000, 256), jnp.float32)
        tbl_21 = 0.05 * jax.random.normal(jax.random.fold_in(_tk, 500 + 21), (12500, 256), jnp.float32)
        tbl_22 = 0.05 * jax.random.normal(jax.random.fold_in(_tk, 500 + 22), (1000, 256), jnp.float32)
        tbl_23 = 0.05 * jax.random.normal(jax.random.fold_in(_tk, 500 + 23), (1000, 256), jnp.float32)
        tbl_24 = 0.05 * jax.random.normal(jax.random.fold_in(_tk, 500 + 24), (1250, 256), jnp.float32)
        tbl_25 = 0.05 * jax.random.normal(jax.random.fold_in(_tk, 500 + 25), (1000, 256), jnp.float32)
        tbl_26 = 0.05 * jax.random.normal(jax.random.fold_in(_tk, 500 + 26), (1000, 256), jnp.float32)
        tbl_27 = 0.05 * jax.random.normal(jax.random.fold_in(_tk, 500 + 27), (12500, 256), jnp.float32)
        tbl_28 = 0.05 * jax.random.normal(jax.random.fold_in(_tk, 500 + 28), (1000, 256), jnp.float32)
        tbl_29 = 0.05 * jax.random.normal(jax.random.fold_in(_tk, 500 + 29), (1250, 256), jnp.float32)
        tbl_30 = 0.05 * jax.random.normal(jax.random.fold_in(_tk, 500 + 30), (1000, 256), jnp.float32)
        tbl_31 = 0.05 * jax.random.normal(jax.random.fold_in(_tk, 500 + 31), (1000, 256), jnp.float32)
        _rk = jax.random.fold_in(_tk, 7)
        W_top1 = 0.0441942 * jax.random.normal(jax.random.fold_in(_tk, 801), (512, 512), jnp.float32)
        W_top2 = 0.0441942 * jax.random.normal(jax.random.fold_in(_tk, 802), (512, 256), jnp.float32)
        W_top3 = 0.0625 * jax.random.normal(jax.random.fold_in(_tk, 803), (256, 1), jnp.float32)
        b_top1 = jnp.zeros((512,), jnp.float32)
        b_top2 = jnp.zeros((256,), jnp.float32)
        return (dense_ctx, ids, tbl_0, tbl_1, tbl_2, tbl_3, tbl_4, tbl_5, tbl_6, tbl_7, tbl_8, tbl_9, tbl_10, tbl_11, tbl_12, tbl_13, tbl_14, tbl_15, tbl_16, tbl_17, tbl_18, tbl_19, tbl_20, tbl_21, tbl_22, tbl_23, tbl_24, tbl_25, tbl_26, tbl_27, tbl_28, tbl_29, tbl_30, tbl_31, W_top1, b_top1, W_top2, b_top2, W_top3)
    dense_ctx, ids, tbl_0, tbl_1, tbl_2, tbl_3, tbl_4, tbl_5, tbl_6, tbl_7, tbl_8, tbl_9, tbl_10, tbl_11, tbl_12, tbl_13, tbl_14, tbl_15, tbl_16, tbl_17, tbl_18, tbl_19, tbl_20, tbl_21, tbl_22, tbl_23, tbl_24, tbl_25, tbl_26, tbl_27, tbl_28, tbl_29, tbl_30, tbl_31, W_top1, b_top1, W_top2, b_top2, W_top3 = _rec_inputs()

    def _L0_rec_setup():
        import jax, jax.numpy as jnp
        import numpy as np
        B, N, D = (1024, 32, 256)
        key = jax.random.key(seed)
        x = jax.random.normal(key, (B, N, D), dtype=jnp.float32)
        return {'x': x}
    _L0_rec_all = _L0_rec_setup()
    _L0_rec_in = {k: v for k, v in _L0_rec_all.items() if k in ()}
    del _L0_rec_all
    return {'dense_ctx': dense_ctx, 'ids': ids, 'tbl_0': tbl_0, 'tbl_1': tbl_1, 'tbl_2': tbl_2, 'tbl_3': tbl_3, 'tbl_4': tbl_4, 'tbl_5': tbl_5, 'tbl_6': tbl_6, 'tbl_7': tbl_7, 'tbl_8': tbl_8, 'tbl_9': tbl_9, 'tbl_10': tbl_10, 'tbl_11': tbl_11, 'tbl_12': tbl_12, 'tbl_13': tbl_13, 'tbl_14': tbl_14, 'tbl_15': tbl_15, 'tbl_16': tbl_16, 'tbl_17': tbl_17, 'tbl_18': tbl_18, 'tbl_19': tbl_19, 'tbl_20': tbl_20, 'tbl_21': tbl_21, 'tbl_22': tbl_22, 'tbl_23': tbl_23, 'tbl_24': tbl_24, 'tbl_25': tbl_25, 'tbl_26': tbl_26, 'tbl_27': tbl_27, 'tbl_28': tbl_28, 'tbl_29': tbl_29, 'tbl_30': tbl_30, 'tbl_31': tbl_31, 'W_top1': W_top1, 'b_top1': b_top1, 'W_top2': W_top2, 'b_top2': b_top2, 'W_top3': W_top3}

def reference(dense_ctx, ids, tbl_0, tbl_1, tbl_2, tbl_3, tbl_4, tbl_5, tbl_6, tbl_7, tbl_8, tbl_9, tbl_10, tbl_11, tbl_12, tbl_13, tbl_14, tbl_15, tbl_16, tbl_17, tbl_18, tbl_19, tbl_20, tbl_21, tbl_22, tbl_23, tbl_24, tbl_25, tbl_26, tbl_27, tbl_28, tbl_29, tbl_30, tbl_31, W_top1, b_top1, W_top2, b_top2, W_top3):
    import jax
    import jax.numpy as jnp

    def _L0_rec_ref(x):
        import jax, jax.numpy as jnp
        import numpy as np
        B, N, D = (1024, 32, 256)
        'Second-order feature interaction (DLRM dot interaction).\n\n            Computes dot(x_i, x_j) for all field pairs i < j (self_interaction=False),\n            flattened in row-major upper-triangular order -> [B, N*(N-1)/2].\n            Matches tf.boolean_mask(dot_products, strictly_upper_mask) ordering.\n            '
        b, n, d = x.shape
        iu, ju = jnp.triu_indices(n, k=1)
        dots = jnp.einsum('bnd,bmd->bnm', x, x)
        return dots[:, iu, ju]
    e = jnp.stack([tbl_0[ids[:, 0]], tbl_1[ids[:, 1]], tbl_2[ids[:, 2]], tbl_3[ids[:, 3]], tbl_4[ids[:, 4]], tbl_5[ids[:, 5]], tbl_6[ids[:, 6]], tbl_7[ids[:, 7]], tbl_8[ids[:, 8]], tbl_9[ids[:, 9]], tbl_10[ids[:, 10]], tbl_11[ids[:, 11]], tbl_12[ids[:, 12]], tbl_13[ids[:, 13]], tbl_14[ids[:, 14]], tbl_15[ids[:, 15]], tbl_16[ids[:, 16]], tbl_17[ids[:, 17]], tbl_18[ids[:, 18]], tbl_19[ids[:, 19]], tbl_20[ids[:, 20]], tbl_21[ids[:, 21]], tbl_22[ids[:, 22]], tbl_23[ids[:, 23]], tbl_24[ids[:, 24]], tbl_25[ids[:, 25]], tbl_26[ids[:, 26]], tbl_27[ids[:, 27]], tbl_28[ids[:, 28]], tbl_29[ids[:, 29]], tbl_30[ids[:, 30]], tbl_31[ids[:, 31]]], axis=1)
    z = _L0_rec_ref(e)
    z = z.reshape(z.shape[0], -1)
    h = jnp.concatenate([z, dense_ctx], axis=1)
    h = jnp.maximum(h @ W_top1 + b_top1, 0.0)
    h = jnp.maximum(h @ W_top2 + b_top2, 0.0)
    y = h @ W_top3
    return y

_drawn_inputs = setup_inputs


def setup_inputs(seed=0):
    import zlib

    import numpy as np

    out = dict(_drawn_inputs(seed))
    spreads = {'b_top1': (0.0, 0.1), 'b_top2': (0.0, 0.1)}
    factors = {}
    for name, (base, spread) in spreads.items():
        noise = np.random.default_rng([zlib.crc32(name.encode()), seed]).standard_normal(out[name].shape)
        drawn = base * np.exp(spread * noise) if base else spread * noise
        out[name] = jnp.asarray(drawn.astype(out[name].dtype))
    for name, factor in factors.items():
        out[name] = (out[name] * factor).astype(out[name].dtype)
    return out
```

```python
import numpy as np

FIELDS = 32
DIM = 256
SAMPLES = 512
DENSE = 16
HIDDEN1 = 512
HIDDEN2 = 256
P = 128
SPG = P // FIELDS
BATCH = 128
BATCHES = SAMPLES // BATCH
GROUPS = BATCH // SPG
QUAD = 4
QUADS = GROUPS // QUAD
HALF = GROUPS // 2
CHUNKS = DIM // P
JO = FIELDS // SPG
QUAD_SAMPLES = QUAD * SPG
M1 = HIDDEN1 // P
M2 = HIDDEN2 // P


def build_program(nc, tables, ids, limits, dense_t, w1_in, b1_in, w2_in, b2_in, w3_in, y_out):
    from contextlib import ExitStack
    import concourse.bass as bass
    import concourse.mybir as mybir

    fp32 = mybir.dt.float32
    int32 = mybir.dt.int32
    ALU = mybir.AluOpType
    ACT = mybir.ActivationFunctionType

    with ExitStack() as ctx:
        def sbuf(name, shape, dtype=fp32):
            return ctx.enter_context(nc.sbuf_tensor(name, shape, dtype))

        def psum(name, shape):
            return ctx.enter_context(nc.psum_tensor(name, shape, fp32))

        def sem(name):
            return ctx.enter_context(nc.semaphore(name))

        ids_sb = sbuf("ids_sb", [P, SAMPLES // SPG], int32)
        limits_sb = sbuf("limits_sb", [P, 2])
        rows = [sbuf(f"rows{h}", [P, HALF], int32) for h in range(2)]
        emb = sbuf("emb", [P, GROUPS, DIM])
        embT = sbuf("embT", [P, 2, CHUNKS, QUAD, P])
        dots = sbuf("dots", [P, JO, BATCH])
        dense = sbuf("dense", [FIELDS, SAMPLES])
        ident = sbuf("ident", [P, P])
        w1 = sbuf("w1", [P, JO, HIDDEN1])
        w2 = sbuf("w2", [P, M1, HIDDEN2])
        w3 = sbuf("w3", [P, M2])
        b1 = sbuf("b1", [P, M1])
        b2 = sbuf("b2", [P, M2])
        h1T = sbuf("h1T", [P, M1, BATCH])
        h2T = sbuf("h2T", [P, M2, BATCH])
        y_sb = sbuf("y_sb", [1, SAMPLES])

        embT_ps = [[psum(f"embT_ps{r}{c}", [P, QUAD, P]) for c in range(CHUNKS)] for r in range(2)]
        gram_ps = [psum(f"gram_ps{r}", [P, QUAD, P]) for r in range(2)]
        mlp_ps = [psum(f"mlp_ps{r}", [P, QUAD, P]) for r in range(2)]
        h1_ps = [ps[:, 0, :] for ps in (*mlp_ps, *gram_ps)]
        h2_ps = [ps[:, 0, :] for ps in mlp_ps]
        y_ps = mlp_ps[0][0:1, 0, :]

        ids_here = sem("ids_here")
        limits_here = sem("limits_here")
        dense_here = sem("dense_here")
        w1_here = sem("w1_here")
        w2_here = sem("w2_here")
        small_here = [sem(n) for n in ("w3_here", "b1_here", "b2_here")]
        pad_zeroed = sem("pad_zeroed")
        ident_zeroed = sem("ident_zeroed")
        ident_ready = sem("ident_ready")
        rows_ready = sem("rows_ready")
        half_begun = sem("half_begun")
        emb_here = [sem(f"emb_here{n}") for n in range(QUADS)]
        transposed = sem("transposed")
        embT_dve = sem("embT_dve")
        embT_act = sem("embT_act")
        gram_done = sem("gram_done")
        dots_dve = sem("dots_dve")
        dots_act = sem("dots_act")
        h1_done = sem("h1_done")
        h1_act = sem("h1_act")
        h1_dve = sem("h1_dve")
        h2_done = sem("h2_done")
        h2_act = sem("h2_act")
        h2_dve = sem("h2_dve")
        y_done = sem("y_done")
        y_ready = sem("y_ready")
        stored = sem("stored")

        block = ctx.enter_context(nc.Block())

        ACT_S = (0,)
        DVE_S = (1, 2, 3)

        def spread(copy, n, s, q, *args):
            first = 1 if q == 0 else 0
            src = gram_ps[n % 2][FIELDS * s:FIELDS * (s + 1), :,
                                 FIELDS * s + JO * q + first:FIELDS * s + JO * (q + 1)]
            at = QUAD_SAMPLES * n + QUAD * s
            dst = dots[FIELDS * q:FIELDS * (q + 1), first:JO, at:at + QUAD]
            return copy(dst, src.rearrange("i g j -> i j g"), *args)

        @block.sync
        def _(sp):
            sp.dma_start(ids_sb[:, :], ids).then_inc(ids_here, 16)
            sp.wait_ge(emb_here[0], 16 * QUAD)
            for j in range(JO):
                sp.dma_start(w1[:, j, :], w1_in[:, j, :]).then_inc(w1_here, 16)
            sp.dma_start(w2[:, :, :], w2_in).then_inc(w2_here, 16)
            sp.wait_ge(pad_zeroed, 1)
            sp.dma_start(dense[0:DENSE, :], dense_t).then_inc(dense_here, 16)
            sp.wait_ge(y_ready, BATCHES)
            sp.dma_start(y_out.rearrange("b a -> a b"), y_sb[:, :]).then_inc(stored, 16)
            sp.wait_ge(stored, 16)

        @block.gpsimd
        def _(pool):
            def gathers(k):
                for h in range(2):
                    pool.wait_ge(rows_ready, 2 * k + h + 1)
                    pool.sem_inc(half_begun, 1)
                    for g in range(HALF):
                        slot = h * HALF + g
                        pool.indirect_dma_start(
                            emb[:, slot, :], None, tables,
                            bass.IndirectOffsetOnAxis(rows[h][:, g:g + 1], 0),
                        ).then_inc(emb_here[slot // QUAD], 16)

            pool.wait_ge(ident_zeroed, 1)
            pool.affine_select(out=ident[:, :], in_=ident[:, :], compare_op=ALU.not_equal, fill=1.0,
                               base=0, pattern=[[-1, P]], channel_multiplier=1).then_inc(ident_ready, 1)
            with pool.Fori(0, BATCHES) as k:
                gathers(k)

        @block.scalar
        def _(act):
            act.dma_start(limits_sb[:, :], limits).then_inc(limits_here, 16)
            for s, dst, src in zip(small_here, (w3, b1, b2), (w3_in, b1_in, b2_in)):
                act.dma_start(dst[:, :], src).then_inc(s, 16)
            act.wait_ge(small_here[1], 16)
            act.wait_ge(small_here[2], 16)

            def take_embT(k, n):
                act.wait_ge(transposed, QUADS * k + n + 1)
                act.activation(embT[:, n % 2, 1, :, :], embT_ps[n % 2][1][:, :, :],
                               ACT.Copy).then_inc(embT_act, 1)

            def place_dots(k, n):
                act.wait_ge(gram_done, QUADS * k + n + 1)
                for s in ACT_S:
                    for q in range(SPG):
                        last = spread(act.activation, n, s, q, ACT.Copy)
                last.then_inc(dots_act, 1)

            def clip_h1(k):
                for m in range(0, M1, 2):
                    act.wait_ge(h1_done, M1 * k + m + 1)
                    act.activation(h1T[:, m, :], h1_ps[m], ACT.Relu,
                                   bias=b1[:, m:m + 1]).then_inc(h1_act, 1)

            def finish(k):
                act.wait_ge(h2_done, M2 * k + 1)
                act.activation(h2T[:, 0, :], h2_ps[0], ACT.Relu, bias=b2[:, 0:1]).then_inc(h2_act, 1)
                act.wait_ge(y_done, k + 1)
                act.activation(y_sb[0:1, bass.ds(BATCH * k, BATCH)], y_ps,
                               ACT.Copy).then_inc(y_ready, 1)

            take_embT(0, 0)
            take_embT(0, 1)
            with act.Fori(0, BATCHES - 1) as k:
                for n in range(QUADS):
                    place_dots(k, n)
                    if n + 2 < QUADS:
                        take_embT(k, n + 2)
                take_embT(k + 1, 0)
                clip_h1(k)
                take_embT(k + 1, 1)
                finish(k)
            k = BATCHES - 1
            for n in range(QUADS):
                place_dots(k, n)
                if n + 2 < QUADS:
                    take_embT(k, n + 2)
            clip_h1(k)
            finish(k)

        @block.vector
        def _(dve):
            dve.memset(ident[:, :], 0.0).then_inc(ident_zeroed, 1)
            dve.memset(dense[:, :], 0.0).then_inc(pad_zeroed, 1)
            dve.wait_ge(ids_here, 16)
            dve.wait_ge(limits_here, 16)

            def stage_rows(k, h):
                dve.tensor_scalar(rows[h][:, :], ids_sb[:, bass.ds(GROUPS * k + HALF * h, HALF)],
                                  limits_sb[:, 0:1], limits_sb[:, 1:2],
                                  ALU.min, ALU.add).then_inc(rows_ready, 1)

            def take_embT(k, n):
                dve.wait_ge(transposed, QUADS * k + n + 1)
                dve.tensor_copy(embT[:, n % 2, 0, :, :], embT_ps[n % 2][0][:, :, :]).then_inc(embT_dve, 1)

            def place_dots(k, n):
                dve.wait_ge(gram_done, QUADS * k + n + 1)
                if n == 0:
                    dve.tensor_copy(dots[0:FIELDS, 0, :], dense[:, bass.ds(BATCH * k, BATCH)])
                for s in DVE_S:
                    for q in range(SPG):
                        last = spread(dve.tensor_copy, n, s, q)
                last.then_inc(dots_dve, 1)

            def clip_h1(k):
                for m in range(1, M1, 2):
                    dve.wait_ge(h1_done, M1 * k + m + 1)
                    dve.tensor_scalar(h1T[:, m, :], h1_ps[m], b1[:, m:m + 1], 0.0,
                                      ALU.add, ALU.max).then_inc(h1_dve, 1)

            def finish(k):
                dve.wait_ge(h2_done, M2 * k + 2)
                dve.tensor_scalar(h2T[:, 1, :], h2_ps[1], b2[:, 1:2], 0.0,
                                  ALU.add, ALU.max).then_inc(h2_dve, 1)

            stage_rows(0, 0)
            stage_rows(0, 1)
            dve.wait_ge(small_here[1], 16)
            dve.wait_ge(small_here[2], 16)
            dve.wait_ge(dense_here, 16)
            take_embT(0, 0)
            take_embT(0, 1)
            with dve.Fori(0, BATCHES - 1) as k:
                for n in range(QUADS):
                    place_dots(k, n)
                    if n + 2 < QUADS:
                        take_embT(k, n + 2)
                        if n + 2 == HALF // QUAD:
                            stage_rows(k + 1, 0)
                        if n + 2 == QUADS - 1:
                            stage_rows(k + 1, 1)
                take_embT(k + 1, 0)
                clip_h1(k)
                take_embT(k + 1, 1)
                finish(k)
            k = BATCHES - 1
            for n in range(QUADS):
                place_dots(k, n)
                if n + 2 < QUADS:
                    take_embT(k, n + 2)
            clip_h1(k)
            finish(k)

        @block.tensor
        def _(pe):
            def transposes(k, n):
                pe.wait_ge(emb_here[n], 16 * QUAD * (k + 1))
                if n >= 2:
                    pe.wait_ge(embT_dve, QUADS * k + n - 1)
                    pe.wait_ge(embT_act, QUADS * k + n - 1)
                for c in range(CHUNKS):
                    for g in range(QUAD):
                        last = pe.transpose(embT_ps[n % 2][c][:, g, :],
                                            emb[:, QUAD * n + g, P * c:P * (c + 1)], ident[:, :])
                last.then_inc(transposed, 1)

            def gram(k, n):
                pe.wait_ge(embT_dve, QUADS * k + n + 1)
                pe.wait_ge(embT_act, QUADS * k + n + 1)
                if n >= 2:
                    pe.wait_ge(dots_dve, QUADS * k + n - 1)
                    pe.wait_ge(dots_act, QUADS * k + n - 1)
                for g in range(QUAD):
                    for c in range(CHUNKS):
                        e = embT[:, n % 2, c, g, :]
                        last = pe.matmul(gram_ps[n % 2][:, g, :], e, e,
                                         start=(c == 0), stop=(c == CHUNKS - 1))
                last.then_inc(gram_done, 1)

            def layer1(k):
                pe.wait_ge(dots_dve, QUADS * (k + 1))
                pe.wait_ge(dots_act, QUADS * (k + 1))
                for m in range(M1):
                    for j in range(JO):
                        last = pe.matmul(h1_ps[m], w1[:, j, P * m:P * (m + 1)], dots[:, j, :],
                                         start=(j == 0), stop=(j == JO - 1))
                    last.then_inc(h1_done, 1)

            def layers23(k):
                for m in range(M2):
                    for c in range(M1):
                        if m == 0:
                            pe.wait_ge((h1_act, h1_dve)[c % 2], M1 // 2 * k + c // 2 + 1)
                        last = pe.matmul(h2_ps[m], w2[:, c, P * m:P * (m + 1)], h1T[:, c, :],
                                         start=(c == 0), stop=(c == M1 - 1))
                    last.then_inc(h2_done, 1)
                for c, ready in enumerate((h2_act, h2_dve)):
                    pe.wait_ge(ready, k + 1)
                    last = pe.matmul(y_ps, w3[:, c:c + 1], h2T[:, c, :],
                                     start=(c == 0), stop=(c == M2 - 1))
                last.then_inc(y_done, 1)

            pe.wait_ge(ident_ready, 1)
            transposes(0, 0)
            transposes(0, 1)
            with pe.Fori(0, BATCHES - 1) as k:
                for n in range(QUADS):
                    gram(k, n)
                    if n + 2 < QUADS:
                        transposes(k, n + 2)
                transposes(k + 1, 0)
                pe.wait_ge(w1_here, 16 * JO)
                pe.wait_ge(w2_here, 16)
                pe.wait_ge(small_here[0], 16)
                layer1(k)
                transposes(k + 1, 1)
                layers23(k)
            k = BATCHES - 1
            for n in range(QUADS):
                gram(k, n)
                if n + 2 < QUADS:
                    transposes(k, n + 2)
            layer1(k)
            layers23(k)


def kernel(**inputs):
    import concourse.bacc as bacc
    from concourse import mybir
    from concourse.bass_utils import run_bass_kernel_spmd

    a = {name: np.asarray(value) for name, value in inputs.items()}
    tables = [a[f"tbl_{f}"] for f in range(FIELDS)]
    heights = np.array([t.shape[0] for t in tables])
    limits = np.stack([np.tile(heights - 1, SPG), np.tile(np.cumsum(heights) - heights, SPG)], axis=1)
    ids = a["ids"].reshape(BATCHES * QUADS, SPG, QUAD, FIELDS).transpose(1, 3, 0, 2).reshape(P, -1)
    w1 = np.zeros((SPG, FIELDS, JO, HIDDEN1), a["W_top1"].dtype)
    first, second = np.triu_indices(FIELDS, 1)
    w1[second // JO, first, second % JO] = a["W_top1"][:len(first)]
    w1[0, :DENSE, 0] = a["W_top1"][len(first):]

    def by_partition(x):
        return x.reshape(-1, P, x.shape[-1]).transpose(1, 0, 2)

    arrays = {
        "tables": np.concatenate(tables, axis=0),
        "ids": ids,
        "limits": limits.astype(np.float32),
        "dense_t": a["dense_ctx"].T,
        "w1": w1.reshape(P, JO, HIDDEN1),
        "b1": a["b_top1"].reshape(M1, P).T,
        "w2": by_partition(a["W_top2"]),
        "b2": a["b_top2"].reshape(M2, P).T,
        "w3": a["W_top3"].reshape(M2, P).T,
    }
    arrays = {name: np.ascontiguousarray(x) for name, x in arrays.items()}
    nc = bacc.Bacc("TRN2", target_bir_lowering=False, num_devices=1)
    t = {name: nc.dram_tensor(f"in_{name}", x.shape, mybir.dt.from_np(x.dtype), kind="ExternalInput").ap()
         for name, x in arrays.items()}
    y = nc.dram_tensor("y", (SAMPLES, 1), mybir.dt.float32, kind="ExternalOutput").ap()
    build_program(nc, t["tables"], t["ids"], t["limits"], t["dense_t"], t["w1"], t["b1"], t["w2"],
                  t["b2"], t["w3"], y)
    r = run_bass_kernel_spmd(nc, [{f"in_{name}": x for name, x in arrays.items()}], core_ids=[0])
    return r.results[0]["y"]
```

```python
import numpy as np

FIELDS = 32
DIM = 256
SAMPLES = 512
DENSE = 16
HIDDEN1 = 512
HIDDEN2 = 256
P = 128
SPG = P // FIELDS
BATCH = 128
BATCHES = SAMPLES // BATCH
GROUPS = BATCH // SPG
QUAD = 4
QUADS = GROUPS // QUAD
PAIR = QUAD // 2
WHOLE = QUADS - 2
PAIRS = (QUADS - WHOLE) * QUAD // PAIR
LAST_UNITS = WHOLE + PAIRS
HALF = GROUPS // 2
CHUNKS = DIM // P
JO = FIELDS // SPG
QUAD_SAMPLES = QUAD * SPG
M1 = HIDDEN1 // P
M2 = HIDDEN2 // P


def build_program(nc, tables, ids, dense_t, w1_in, b1_in, w2_in, b2_in, w3_in, y_out):
    from contextlib import ExitStack
    import concourse.bass as bass
    import concourse.mybir as mybir

    fp32 = mybir.dt.float32
    int32 = mybir.dt.int32
    ALU = mybir.AluOpType
    ACT = mybir.ActivationFunctionType

    with ExitStack() as ctx:
        def sbuf(name, shape, dtype=fp32):
            return ctx.enter_context(nc.sbuf_tensor(name, shape, dtype))

        def psum(name, shape):
            return ctx.enter_context(nc.psum_tensor(name, shape, fp32))

        def sem(name):
            return ctx.enter_context(nc.semaphore(name))

        ids_sb = sbuf("ids_sb", [P, SAMPLES // SPG + 2], int32)
        last_row = ids_sb[:, SAMPLES // SPG:SAMPLES // SPG + 1]
        first_row = ids_sb[:, SAMPLES // SPG + 1:SAMPLES // SPG + 2]
        rows = [sbuf(f"rows{h}", [P, HALF], int32) for h in range(2)]
        emb = sbuf("emb", [P, GROUPS, DIM])
        embT = sbuf("embT", [P, 2, CHUNKS, QUAD, P])
        dots = sbuf("dots", [P, JO, BATCH])
        dense = sbuf("dense", [FIELDS, SAMPLES])
        ident = sbuf("ident", [P, P])
        w1 = sbuf("w1", [P, JO, HIDDEN1])
        w2 = sbuf("w2", [P, M1, HIDDEN2])
        w3 = sbuf("w3", [P, M2])
        b1 = sbuf("b1", [P, M1])
        b2 = sbuf("b2", [P, M2])
        h1T = sbuf("h1T", [P, M1, BATCH])
        h2T = sbuf("h2T", [P, M2, BATCH])
        y_sb = sbuf("y_sb", [1, SAMPLES])

        embT_ps = [[psum(f"embT_ps{r}{c}", [P, QUAD, P]) for c in range(CHUNKS)] for r in range(2)]
        gram_ps = [psum(f"gram_ps{r}", [P, QUAD, P]) for r in range(2)]
        mlp_ps = [psum(f"mlp_ps{r}", [P, QUAD, P]) for r in range(2)]
        h1_ps = [ps[:, 0, :] for ps in (*mlp_ps, *gram_ps)]
        h2_ps = [ps[:, 0, :] for ps in mlp_ps]
        y_ps = mlp_ps[0][0:1, 0, :]

        ids_here = sem("ids_here")
        dense_here = sem("dense_here")
        w1_here = sem("w1_here")
        w2_here = sem("w2_here")
        small_here = [sem(n) for n in ("w3_here", "b1_here", "b2_here")]
        pad_zeroed = sem("pad_zeroed")
        ident_zeroed = sem("ident_zeroed")
        ident_ready = sem("ident_ready")
        rows_ready = sem("rows_ready")
        emb_pair = [sem(f"emb_pair{n}") for n in range(PAIRS)]
        half_begun = sem("half_begun")
        emb_here = [sem(f"emb_here{n}") for n in range(QUADS)]
        transposed = sem("transposed")
        embT_dve = sem("embT_dve")
        embT_act = sem("embT_act")
        gram_done = sem("gram_done")
        dots_dve = sem("dots_dve")
        dots_act = sem("dots_act")
        h1_done = sem("h1_done")
        h1_act = sem("h1_act")
        h1_dve = sem("h1_dve")
        h2_done = sem("h2_done")
        h2_act = sem("h2_act")
        h2_dve = sem("h2_dve")
        y_done = sem("y_done")
        y_ready = sem("y_ready")
        stored = sem("stored")

        block = ctx.enter_context(nc.Block())

        ACT_S = (0, 1)
        DVE_S = (2, 3)

        def unit(k, n):
            if isinstance(k, int) and k == BATCHES - 1 and n >= WHOLE:
                return QUAD * WHOLE + PAIR * (n - WHOLE), PAIR
            return QUAD * n, QUAD

        def spread(copy, k, n, s, q, *args):
            g, size = unit(k, n)
            first = 1 if q == 0 else 0
            src = gram_ps[n % 2][FIELDS * s:FIELDS * (s + 1), 0:size,
                                 FIELDS * s + JO * q + first:FIELDS * s + JO * (q + 1)]
            at = QUAD_SAMPLES * (g // QUAD) + QUAD * s + g % QUAD
            dst = dots[FIELDS * q:FIELDS * (q + 1), first:JO, at:at + size]
            return copy(dst, src.rearrange("i g j -> i j g"), *args)

        @block.sync
        def _(sp):
            sp.dma_start(ids_sb[:, :], ids).then_inc(ids_here, 16)
            sp.wait_ge(emb_here[0], 16 * QUAD)
            for j in range(JO):
                sp.dma_start(w1[:, j, :], w1_in[:, j, :]).then_inc(w1_here, 16)
            sp.dma_start(w2[:, :, :], w2_in).then_inc(w2_here, 16)
            sp.wait_ge(pad_zeroed, 1)
            sp.dma_start(dense[0:DENSE, :], dense_t).then_inc(dense_here, 16)
            sp.wait_ge(y_ready, BATCHES)
            sp.dma_start(y_out.rearrange("b a -> a b"), y_sb[:, :]).then_inc(stored, 16)
            sp.wait_ge(stored, 16)

        @block.gpsimd
        def _(pool):
            def signal(k, slot):
                if isinstance(k, int) and slot >= QUAD * WHOLE:
                    return emb_pair[(slot - QUAD * WHOLE) // PAIR]
                return emb_here[slot // QUAD]

            def gathers(k):
                for h in range(2):
                    pool.wait_ge(rows_ready, 2 * k + h + 1)
                    pool.sem_inc(half_begun, 1)
                    for g in range(HALF):
                        slot = h * HALF + g
                        pool.indirect_dma_start(
                            emb[:, slot, :], None, tables,
                            bass.IndirectOffsetOnAxis(rows[h][:, g:g + 1], 0),
                        ).then_inc(signal(k, slot), 16)

            pool.wait_ge(ident_zeroed, 1)
            pool.affine_select(out=ident[:, :], in_=ident[:, :], compare_op=ALU.not_equal, fill=1.0,
                               base=0, pattern=[[-1, P]], channel_multiplier=1).then_inc(ident_ready, 1)
            with pool.Fori(0, BATCHES - 1) as k:
                gathers(k)
            gathers(BATCHES - 1)

        @block.scalar
        def _(act):
            for s, dst, src in zip(small_here, (w3, b1, b2), (w3_in, b1_in, b2_in)):
                act.dma_start(dst[:, :], src).then_inc(s, 16)
            act.wait_ge(small_here[1], 16)
            act.wait_ge(small_here[2], 16)

            def take_embT(k, n):
                act.wait_ge(transposed, QUADS * k + n + 1)
                size = unit(k, n)[1]
                act.activation(embT[:, n % 2, 1, 0:size, :], embT_ps[n % 2][1][:, 0:size, :],
                               ACT.Copy).then_inc(embT_act, 1)

            def place_dots(k, n):
                act.wait_ge(gram_done, QUADS * k + n + 1)
                for s in ACT_S:
                    for q in range(SPG):
                        last = spread(act.activation, k, n, s, q, ACT.Copy)
                last.then_inc(dots_act, 1)

            def clip_h1(k):
                for m in range(0, M1, 2):
                    act.wait_ge(h1_done, M1 * k + m + 1)
                    act.activation(h1T[:, m, :], h1_ps[m], ACT.Relu,
                                   bias=b1[:, m:m + 1]).then_inc(h1_act, 1)

            def finish(k):
                act.wait_ge(h2_done, M2 * k + 1)
                act.activation(h2T[:, 0, :], h2_ps[0], ACT.Relu, bias=b2[:, 0:1]).then_inc(h2_act, 1)
                act.wait_ge(y_done, k + 1)
                act.activation(y_sb[0:1, bass.ds(BATCH * k, BATCH)], y_ps,
                               ACT.Copy).then_inc(y_ready, 1)

            take_embT(0, 0)
            take_embT(0, 1)
            with act.Fori(0, BATCHES - 1) as k:
                for n in range(QUADS):
                    place_dots(k, n)
                    if n + 2 < QUADS:
                        take_embT(k, n + 2)
                take_embT(k + 1, 0)
                clip_h1(k)
                take_embT(k + 1, 1)
                finish(k)
            k = BATCHES - 1
            for n in range(LAST_UNITS):
                place_dots(k, n)
                if n + 2 < LAST_UNITS:
                    take_embT(k, n + 2)
            clip_h1(k)
            finish(k)

        @block.vector
        def _(dve):
            dve.memset(ident[:, :], 0.0).then_inc(ident_zeroed, 1)
            dve.memset(dense[:, :], 0.0).then_inc(pad_zeroed, 1)
            dve.wait_ge(ids_here, 16)

            def stage_rows(k, h):
                dve.tensor_scalar(rows[h][:, :], ids_sb[:, bass.ds(GROUPS * k + HALF * h, HALF)],
                                  last_row, first_row,
                                  ALU.min, ALU.add).then_inc(rows_ready, 1)

            def take_embT(k, n):
                dve.wait_ge(transposed, QUADS * k + n + 1)
                size = unit(k, n)[1]
                dve.tensor_copy(embT[:, n % 2, 0, 0:size, :],
                                embT_ps[n % 2][0][:, 0:size, :]).then_inc(embT_dve, 1)

            def place_dots(k, n):
                dve.wait_ge(gram_done, QUADS * k + n + 1)
                if n == 0:
                    dve.tensor_copy(dots[0:FIELDS, 0, :], dense[:, bass.ds(BATCH * k, BATCH)])
                for s in DVE_S:
                    for q in range(SPG):
                        last = spread(dve.tensor_copy, k, n, s, q)
                last.then_inc(dots_dve, 1)

            def clip_h1(k):
                for m in range(1, M1, 2):
                    dve.wait_ge(h1_done, M1 * k + m + 1)
                    dve.tensor_scalar(h1T[:, m, :], h1_ps[m], b1[:, m:m + 1], 0.0,
                                      ALU.add, ALU.max).then_inc(h1_dve, 1)

            def finish(k):
                dve.wait_ge(h2_done, M2 * k + 2)
                dve.tensor_scalar(h2T[:, 1, :], h2_ps[1], b2[:, 1:2], 0.0,
                                  ALU.add, ALU.max).then_inc(h2_dve, 1)

            stage_rows(0, 0)
            stage_rows(0, 1)
            dve.wait_ge(small_here[1], 16)
            dve.wait_ge(small_here[2], 16)
            dve.wait_ge(dense_here, 16)
            take_embT(0, 0)
            take_embT(0, 1)
            with dve.Fori(0, BATCHES - 1) as k:
                for n in range(QUADS):
                    place_dots(k, n)
                    if n + 2 < QUADS:
                        take_embT(k, n + 2)
                        if n + 2 == HALF // QUAD:
                            stage_rows(k + 1, 0)
                        if n + 2 == QUADS - 1:
                            stage_rows(k + 1, 1)
                take_embT(k + 1, 0)
                clip_h1(k)
                take_embT(k + 1, 1)
                finish(k)
            k = BATCHES - 1
            for n in range(LAST_UNITS):
                place_dots(k, n)
                if n + 2 < LAST_UNITS:
                    take_embT(k, n + 2)
            clip_h1(k)
            finish(k)

        @block.tensor
        def _(pe):
            def transposes(k, n):
                first, size = unit(k, n)
                if size == PAIR:
                    pe.wait_ge(emb_pair[n - WHOLE], 16 * PAIR)
                else:
                    pe.wait_ge(emb_here[n], 16 * QUAD * (k + 1))
                if n >= 2:
                    pe.wait_ge(embT_dve, QUADS * k + n - 1)
                    pe.wait_ge(embT_act, QUADS * k + n - 1)
                for c in range(CHUNKS):
                    for g in range(size):
                        last = pe.transpose(embT_ps[n % 2][c][:, g, :],
                                            emb[:, first + g, P * c:P * (c + 1)], ident[:, :])
                last.then_inc(transposed, 1)

            def gram(k, n):
                pe.wait_ge(embT_dve, QUADS * k + n + 1)
                pe.wait_ge(embT_act, QUADS * k + n + 1)
                if n >= 2:
                    pe.wait_ge(dots_dve, QUADS * k + n - 1)
                    pe.wait_ge(dots_act, QUADS * k + n - 1)
                for g in range(unit(k, n)[1]):
                    for c in range(CHUNKS):
                        e = embT[:, n % 2, c, g, :]
                        last = pe.matmul(gram_ps[n % 2][:, g, :], e, e,
                                         start=(c == 0), stop=(c == CHUNKS - 1))
                last.then_inc(gram_done, 1)

            def layer1(k, units):
                pe.wait_ge(dots_dve, QUADS * k + units)
                pe.wait_ge(dots_act, QUADS * k + units)
                for m in range(M1):
                    for j in range(JO):
                        last = pe.matmul(h1_ps[m], w1[:, j, P * m:P * (m + 1)], dots[:, j, :],
                                         start=(j == 0), stop=(j == JO - 1))
                    last.then_inc(h1_done, 1)

            def layers23(k):
                for m in range(M2):
                    for c in range(M1):
                        if m == 0:
                            pe.wait_ge((h1_act, h1_dve)[c % 2], M1 // 2 * k + c // 2 + 1)
                        last = pe.matmul(h2_ps[m], w2[:, c, P * m:P * (m + 1)], h1T[:, c, :],
                                         start=(c == 0), stop=(c == M1 - 1))
                    last.then_inc(h2_done, 1)
                for c, ready in enumerate((h2_act, h2_dve)):
                    pe.wait_ge(ready, k + 1)
                    last = pe.matmul(y_ps, w3[:, c:c + 1], h2T[:, c, :],
                                     start=(c == 0), stop=(c == M2 - 1))
                last.then_inc(y_done, 1)

            pe.wait_ge(ident_ready, 1)
            transposes(0, 0)
            transposes(0, 1)
            with pe.Fori(0, BATCHES - 1) as k:
                for n in range(QUADS):
                    gram(k, n)
                    if n + 2 < QUADS:
                        transposes(k, n + 2)
                transposes(k + 1, 0)
                pe.wait_ge(w1_here, 16 * JO)
                pe.wait_ge(w2_here, 16)
                pe.wait_ge(small_here[0], 16)
                layer1(k, QUADS)
                transposes(k + 1, 1)
                layers23(k)
            k = BATCHES - 1
            for n in range(LAST_UNITS):
                gram(k, n)
                if n + 2 < LAST_UNITS:
                    transposes(k, n + 2)
            layer1(k, LAST_UNITS)
            layers23(k)


def kernel(**inputs):
    import concourse.bacc as bacc
    from concourse import mybir
    from concourse.bass_utils import run_bass_kernel_spmd

    a = {name: np.asarray(value) for name, value in inputs.items()}
    tables = [a[f"tbl_{f}"] for f in range(FIELDS)]
    ids_in = a["ids"]
    heights = np.array([t.shape[0] for t in tables])
    limits = np.stack([np.tile(heights - 1, SPG), np.tile(np.cumsum(heights) - heights, SPG)], axis=1)
    limits = limits.astype(ids_in.dtype)
    ids = ids_in.reshape(BATCHES * QUADS, SPG, QUAD, FIELDS).transpose(1, 3, 0, 2).reshape(P, -1)
    w1 = np.zeros((SPG, FIELDS, JO, HIDDEN1), a["W_top1"].dtype)
    first, second = np.triu_indices(FIELDS, 1)
    w1[second // JO, first, second % JO] = a["W_top1"][:len(first)]
    w1[0, :DENSE, 0] = a["W_top1"][len(first):]

    def by_partition(x):
        return x.reshape(-1, P, x.shape[-1]).transpose(1, 0, 2)

    arrays = {
        "tables": np.concatenate(tables, axis=0),
        "ids": np.concatenate([ids, limits], axis=1),
        "dense_t": a["dense_ctx"].T,
        "w1": w1.reshape(P, JO, HIDDEN1),
        "b1": a["b_top1"].reshape(M1, P).T,
        "w2": by_partition(a["W_top2"]),
        "b2": a["b_top2"].reshape(M2, P).T,
        "w3": a["W_top3"].reshape(M2, P).T,
    }
    arrays = {name: np.ascontiguousarray(x) for name, x in arrays.items()}
    nc = bacc.Bacc("TRN2", target_bir_lowering=False, num_devices=1)
    t = {name: nc.dram_tensor(f"in_{name}", x.shape, mybir.dt.from_np(x.dtype), kind="ExternalInput").ap()
         for name, x in arrays.items()}
    y = nc.dram_tensor("y", (SAMPLES, 1), mybir.dt.float32, kind="ExternalOutput").ap()
    build_program(nc, t["tables"], t["ids"], t["dense_t"], t["w1"], t["b1"], t["w2"],
                  t["b2"], t["w3"], y)
    r = run_bass_kernel_spmd(nc, [{f"in_{name}": x for name, x in arrays.items()}], core_ids=[0])
    return r.results[0]["y"]
```
